# Optimizing a Trainium2 kernel written in Bass

```python
import numpy as np
import jax
import jax.numpy as jnp

def _softmax(x, axis=-1):
    return jax.nn.softmax(x, axis=axis)

def _gelu(x):
    return jax.nn.gelu(x, approximate=True)

def _silu(x):
    return jax.nn.silu(x)

def _sigmoid(x):
    return jax.nn.sigmoid(x)

def _layernorm(x, axis=-1, eps=1e-05):
    m = jnp.mean(x, axis=axis, keepdims=True)
    v = jnp.var(x, axis=axis, keepdims=True)
    return (x - m) / jnp.sqrt(v + eps)

def _scatter_add(tgt, idx, src, axis=0):
    return tgt.at[idx].add(src)

def _segment_sum(src, seg, n):
    return jax.ops.segment_sum(src, seg, n)
kernel_name = 'mk_dlrm_tower_d1_rec_r8_6d6032'

def setup_inputs(seed: int=0):
    np.random.seed(seed)
    _w = jnp.asarray

    def _rec_inputs():
        import jax
        import jax.numpy as jnp
        _tk = jax.random.key(seed)
        dense_ctx = jax.random.normal(jax.random.fold_in(_tk, 190), (1024, 16), jnp.float32)
        ids = jnp.stack([jax.random.randint(jax.random.fold_in(_tk, 200 + f), (1024,), 0, v, jnp.int32) for f, v in enumerate([12500, 12500, 125000, 125000, 12500, 1000, 12500, 1000, 125000, 1000, 125000, 12500, 12500, 12500, 125000, 1250, 125000, 1000, 1250, 12500, 125000, 1250, 1250, 125000, 125000, 125000, 1250, 125000, 1000, 1250, 1250, 12500, 125000, 1250, 1250, 12500, 1250, 125000, 1000])], axis=1)
        tbl_0 = 0.05 * jax.random.normal(jax.random.fold_in(_tk, 500 + 0), (12500, 16), jnp.float32)
        tbl_1 = 0.05 * jax.random.normal(jax.random.fold_in(_tk, 500 + 1), (12500, 16), jnp.float32)
        tbl_2 = 0.05 * jax.random.normal(jax.random.fold_in(_tk, 500 + 2), (125000, 16), jnp.float32)
        tbl_3 = 0.05 * jax.random.normal(jax.random.fold_in(_tk, 500 + 3), (125000, 16), jnp.float32)
        tbl_4 = 0.05 * jax.random.normal(jax.random.fold_in(_tk, 500 + 4), (12500, 16), jnp.float32)
        tbl_5 = 0.05 * jax.random.normal(jax.random.fold_in(_tk, 500 + 5), (1000, 16), jnp.float32)
        tbl_6 = 0.05 * jax.random.normal(jax.random.fold_in(_tk, 500 + 6), (12500, 16), jnp.float32)
        tbl_7 = 0.05 * jax.random.normal(jax.random.fold_in(_tk, 500 + 7), (1000, 16), jnp.float32)
        tbl_8 = 0.05 * jax.random.normal(jax.random.fold_in(_tk, 500 + 8), (125000, 16), jnp.float32)
        tbl_9 = 0.05 * jax.random.normal(jax.random.fold_in(_tk, 500 + 9), (1000, 16), jnp.float32)
        tbl_10 = 0.05 * jax.random.normal(jax.random.fold_in(_tk, 500 + 10), (125000, 16), jnp.float32)
        tbl_11 = 0.05 * jax.random.normal(jax.random.fold_in(_tk, 500 + 11), (12500, 16), jnp.float32)
        tbl_12 = 0.05 * jax.random.normal(jax.random.fold_in(_tk, 500 + 12), (12500, 16), jnp.float32)
        tbl_13 = 0.05 * jax.random.normal(jax.random.fold_in(_tk, 500 + 13), (12500, 16), jnp.float32)
        tbl_14 = 0.05 * jax.random.normal(jax.random.fold_in(_tk, 500 + 14), (125000, 16), jnp.float32)
        tbl_15 = 0.05 * jax.random.normal(jax.random.fold_in(_tk, 500 + 15), (1250, 16), jnp.float32)
        tbl_16 = 0.05 * jax.random.normal(jax.random.fold_in(_tk, 500 + 16), (125000, 16), jnp.float32)
        tbl_17 = 0.05 * jax.random.normal(jax.random.fold_in(_tk, 500 + 17), (1000, 16), jnp.float32)
        tbl_18 = 0.05 * jax.random.normal(jax.random.fold_in(_tk, 500 + 18), (1250, 16), jnp.float32)
        tbl_19 = 0.05 * jax.random.normal(jax.random.fold_in(_tk, 500 + 19), (12500, 16), jnp.float32)
        tbl_20 = 0.05 * jax.random.normal(jax.random.fold_in(_tk, 500 + 20), (125000, 16), jnp.float32)
        tbl_21 = 0.05 * jax.random.normal(jax.random.fold_in(_tk, 500 + 21), (1250, 16), jnp.float32)
        tbl_22 = 0.05 * jax.random.normal(jax.random.fold_in(_tk, 500 + 22), (1250, 16), jnp.float32)
        tbl_23 = 0.05 * jax.random.normal(jax.random.fold_in(_tk, 500 + 23), (125000, 16), jnp.float32)
        tbl_24 = 0.05 * jax.random.normal(jax.random.fold_in(_tk, 500 + 24), (125000, 16), jnp.float32)
        tbl_25 = 0.05 * jax.random.normal(jax.random.fold_in(_tk, 500 + 25), (125000, 16), jnp.float32)
        tbl_26 = 0.05 * jax.random.normal(jax.random.fold_in(_tk, 500 + 26), (1250, 16), jnp.float32)
        tbl_27 = 0.05 * jax.random.normal(jax.random.fold_in(_tk, 500 + 27), (125000, 16), jnp.float32)
        tbl_28 = 0.05 * jax.random.normal(jax.random.fold_in(_tk, 500 + 28), (1000, 16), jnp.float32)
        tbl_29 = 0.05 * jax.random.normal(jax.random.fold_in(_tk, 500 + 29), (1250, 16), jnp.float32)
        tbl_30 = 0.05 * jax.random.normal(jax.random.fold_in(_tk, 500 + 30), (1250, 16), jnp.float32)
        tbl_31 = 0.05 * jax.random.normal(jax.random.fold_in(_tk, 500 + 31), (12500, 16), jnp.float32)
        tbl_32 = 0.05 * jax.random.normal(jax.random.fold_in(_tk, 500 + 32), (125000, 16), jnp.float32)
        tbl_33 = 0.05 * jax.random.normal(jax.random.fold_in(_tk, 500 + 33), (1250, 16), jnp.float32)
        tbl_34 = 0.05 * jax.random.normal(jax.random.fold_in(_tk, 500 + 34), (1250, 16), jnp.float32)
        tbl_35 = 0.05 * jax.random.normal(jax.random.fold_in(_tk, 500 + 35), (12500, 16), jnp.float32)
        tbl_36 = 0.05 * jax.random.normal(jax.random.fold_in(_tk, 500 + 36), (1250, 16), jnp.float32)
        tbl_37 = 0.05 * jax.random.normal(jax.random.fold_in(_tk, 500 + 37), (125000, 16), jnp.float32)
        tbl_38 = 0.05 * jax.random.normal(jax.random.fold_in(_tk, 500 + 38), (1000, 16), jnp.float32)
        _rk = jax.random.fold_in(_tk, 7)
        W_top1 = 0.0606339 * jax.random.normal(jax.random.fold_in(_tk, 801), (272, 512), jnp.float32)
        W_top2 = 0.0441942 * jax.random.normal(jax.random.fold_in(_tk, 802), (512, 256), jnp.float32)
        W_top3 = 0.0625 * jax.random.normal(jax.random.fold_in(_tk, 803), (256, 1), jnp.float32)
        b_top1 = jnp.zeros((512,), jnp.float32)
        b_top2 = jnp.zeros((256,), jnp.float32)
        return (dense_ctx, ids, tbl_0, tbl_1, tbl_2, tbl_3, tbl_4, tbl_5, tbl_6, tbl_7, tbl_8, tbl_9, tbl_10, tbl_11, tbl_12, tbl_13, tbl_14, tbl_15, tbl_16, tbl_17, tbl_18, tbl_19, tbl_20, tbl_21, tbl_22, tbl_23, tbl_24, tbl_25, tbl_26, tbl_27, tbl_28, tbl_29, tbl_30, tbl_31, tbl_32, tbl_33, tbl_34, tbl_35, tbl_36, tbl_37, tbl_38, W_top1, b_top1, W_top2, b_top2, W_top3)
    dense_ctx, ids, tbl_0, tbl_1, tbl_2, tbl_3, tbl_4, tbl_5, tbl_6, tbl_7, tbl_8, tbl_9, tbl_10, tbl_11, tbl_12, tbl_13, tbl_14, tbl_15, tbl_16, tbl_17, tbl_18, tbl_19, tbl_20, tbl_21, tbl_22, tbl_23, tbl_24, tbl_25, tbl_26, tbl_27, tbl_28, tbl_29, tbl_30, tbl_31, tbl_32, tbl_33, tbl_34, tbl_35, tbl_36, tbl_37, tbl_38, W_top1, b_top1, W_top2, b_top2, W_top3 = _rec_inputs()

    def _L0_rec_setup():
        import jax, jax.numpy as jnp
        import numpy as np
        B, F0, D = (256, 39, 16)
        H1, H2 = (128, 128)
        key = jax.random.key(seed)
        k1, k2, k3 = jax.random.split(key, 3)
        x = jax.random.normal(k1, (B, F0, D), dtype=jnp.float32)

        def xavier(k, out_c, in_c):
            bound = np.sqrt(6.0 / (in_c + out_c)).astype(np.float32)
            return jax.random.uniform(k, (out_c, in_c, 1), dtype=jnp.float32, minval=-bound, maxval=bound)
        W0 = xavier(k2, H1, F0 * F0)
        W1 = xavier(k3, H2, F0 * H1)
        return {'input': x, 'W0': W0, 'W1': W1}
    _L0_rec_all = _L0_rec_setup()
    _L0_rec_in = {k: v for k, v in _L0_rec_all.items() if k in ('W0', 'W1')}
    del _L0_rec_all
    return {'dense_ctx': dense_ctx, 'ids': ids, 'tbl_0': tbl_0, 'tbl_1': tbl_1, 'tbl_2': tbl_2, 'tbl_3': tbl_3, 'tbl_4': tbl_4, 'tbl_5': tbl_5, 'tbl_6': tbl_6, 'tbl_7': tbl_7, 'tbl_8': tbl_8, 'tbl_9': tbl_9, 'tbl_10': tbl_10, 'tbl_11': tbl_11, 'tbl_12': tbl_12, 'tbl_13': tbl_13, 'tbl_14': tbl_14, 'tbl_15': tbl_15, 'tbl_16': tbl_16, 'tbl_17': tbl_17, 'tbl_18': tbl_18, 'tbl_19': tbl_19, 'tbl_20': tbl_20, 'tbl_21': tbl_21, 'tbl_22': tbl_22, 'tbl_23': tbl_23, 'tbl_24': tbl_24, 'tbl_25': tbl_25, 'tbl_26': tbl_26, 'tbl_27': tbl_27, 'tbl_28': tbl_28, 'tbl_29': tbl_29, 'tbl_30': tbl_30, 'tbl_31': tbl_31, 'tbl_32': tbl_32, 'tbl_33': tbl_33, 'tbl_34': tbl_34, 'tbl_35': tbl_35, 'tbl_36': tbl_36, 'tbl_37': tbl_37, 'tbl_38': tbl_38, 'W_top1': W_top1, 'b_top1': b_top1, 'W_top2': W_top2, 'b_top2': b_top2, 'W_top3': W_top3, 'L0_rec_W0': _L0_rec_in['W0'], 'L0_rec_W1': _L0_rec_in['W1']}

def reference(dense_ctx, ids, tbl_0, tbl_1, tbl_2, tbl_3, tbl_4, tbl_5, tbl_6, tbl_7, tbl_8, tbl_9, tbl_10, tbl_11, tbl_12, tbl_13, tbl_14, tbl_15, tbl_16, tbl_17, tbl_18, tbl_19, tbl_20, tbl_21, tbl_22, tbl_23, tbl_24, tbl_25, tbl_26, tbl_27, tbl_28, tbl_29, tbl_30, tbl_31, tbl_32, tbl_33, tbl_34, tbl_35, tbl_36, tbl_37, tbl_38, W_top1, b_top1, W_top2, b_top2, W_top3, L0_rec_W0, L0_rec_W1):
    import jax
    import jax.numpy as jnp

    def _L0_rec_ref(input, W0, W1):
        import jax, jax.numpy as jnp
        import numpy as np
        B, F0, D = (256, 39, 16)
        H1, H2 = (128, 128)
        x0 = input
        h = input
        outs = []
        for W in (W0, W1):
            Hout, P, _ = W.shape
            Hk = h.shape[1]
            Wr = W[:, :, 0].reshape(Hout, x0.shape[1], Hk)
            h = jnp.einsum('bfd,bqd,hfq->bhd', x0, h, Wr)
            outs.append(h)
        result = jnp.concatenate(outs, axis=1)
        return jnp.sum(result, axis=2)
    e = jnp.stack([tbl_0[ids[:, 0]], tbl_1[ids[:, 1]], tbl_2[ids[:, 2]], tbl_3[ids[:, 3]], tbl_4[ids[:, 4]], tbl_5[ids[:, 5]], tbl_6[ids[:, 6]], tbl_7[ids[:, 7]], tbl_8[ids[:, 8]], tbl_9[ids[:, 9]], tbl_10[ids[:, 10]], tbl_11[ids[:, 11]], tbl_12[ids[:, 12]], tbl_13[ids[:, 13]], tbl_14[ids[:, 14]], tbl_15[ids[:, 15]], tbl_16[ids[:, 16]], tbl_17[ids[:, 17]], tbl_18[ids[:, 18]], tbl_19[ids[:, 19]], tbl_20[ids[:, 20]], tbl_21[ids[:, 21]], tbl_22[ids[:, 22]], tbl_23[ids[:, 23]], tbl_24[ids[:, 24]], tbl_25[ids[:, 25]], tbl_26[ids[:, 26]], tbl_27[ids[:, 27]], tbl_28[ids[:, 28]], tbl_29[ids[:, 29]], tbl_30[ids[:, 30]], tbl_31[ids[:, 31]], tbl_32[ids[:, 32]], tbl_33[ids[:, 33]], tbl_34[ids[:, 34]], tbl_35[ids[:, 35]], tbl_36[ids[:, 36]], tbl_37[ids[:, 37]], tbl_38[ids[:, 38]]], axis=1)
    z = _L0_rec_ref(e, L0_rec_W0, L0_rec_W1)
    z = z.reshape(z.shape[0], -1)
    h = jnp.concatenate([z, dense_ctx], axis=1)
    h = jnp.maximum(h @ W_top1 + b_top1, 0.0)
    h = jnp.maximum(h @ W_top2 + b_top2, 0.0)
    y = h @ W_top3
    return y

_drawn_inputs = setup_inputs


def setup_inputs(seed=0):
    import zlib

    import numpy as np

    out = dict(_drawn_inputs(seed))
    spreads = {'b_top1': (0.0, 0.1), 'b_top2': (0.0, 0.1)}
    factors = {'tbl_0': 7.014,
     'tbl_1': 6.274,
     'tbl_2': 6.777,
     'tbl_3': 6.889,
     'tbl_4': 7.082,
     'tbl_5': 7.082,
     'tbl_6': 6.816,
     'tbl_7': 7.695,
     'tbl_8': 7.242,
     'tbl_9': 7.457,
     'tbl_10': 7.031,
     'tbl_11': 7.083,
     'tbl_12': 7.2,
     'tbl_13': 7.364,
     'tbl_14': 7.03,
     'tbl_15': 7.373,
     'tbl_16': 6.505,
     'tbl_17': 7.726,
     'tbl_18': 6.969,
     'tbl_19': 7.677,
     'tbl_20': 6.594,
     'tbl_21': 7.576,
     'tbl_22': 7.364,
     'tbl_23': 7.458,
     'tbl_24': 6.457,
     'tbl_25': 7.129,
     'tbl_26': 7.292,
     'tbl_27': 7.117,
     'tbl_28': 7.108,
     'tbl_29': 7.186,
     'tbl_30': 6.646,
     'tbl_31': 6.773,
     'tbl_32': 7.242,
     'tbl_33': 7.272,
     'tbl_34': 6.963,
     'tbl_35': 6.959,
     'tbl_36': 7.496,
     'tbl_37': 6.748,
     'tbl_38': 7.009,
     'L0_rec_W1': 8.0}
    for name, (base, spread) in spreads.items():
        noise = np.random.default_rng([zlib.crc32(name.encode()), seed]).standard_normal(out[name].shape)
        drawn = base * np.exp(spread * noise) if base else spread * noise
        out[name] = jnp.asarray(drawn.astype(out[name].dtype))
    for name, factor in factors.items():
        out[name] = (out[name] * factor).astype(out[name].dtype)
    return out
```

```python
from contextlib import ExitStack

import concourse.bass as bass
from concourse import mybir

F32 = mybir.dt.float32
BF16 = mybir.dt.bfloat16
I32 = mybir.dt.int32
ALU = mybir.AluOpType
ACT = mybir.ActivationFunctionType

P = 128
PARTS = 3
SHIFTS = 3
RING = 4
BATCHES = (6, 5, 5)


def build(nc, dense, ids, tables, w_top1, b_top1, w_top2, b_top2, w_top3, w0, w1, out):
    NB, NF = ids.shape
    D = tables[0].shape[1]
    H = w0.shape[0]
    ND = dense.shape[1]
    M1, M2 = w_top2.shape
    TILES = NB // P
    KR = SHIFTS * NF
    NSHIFT = NF // 2 + 1
    CHUNKS = -(-NSHIFT // SHIFTS)
    rows = [min(SHIFTS, NSHIFT - SHIFTS * j) * NF for j in range(CHUNKS)]
    COL = 512
    SB = COL // D
    BLOCKS = P // SB
    GROUPS = P // 8
    GF = NF + 1
    PT = BLOCKS * CHUNKS
    assert NF % 2 == 1 and D == 16 and H == P and TILES % 2 == 0 and PT % RING == 0

    items = [("A", 0)]
    for c in range(BLOCKS):
        for j in range(CHUNKS):
            items.append(("B", c, j))
            if j == 2 and c + 1 < BLOCKS:
                items.append(("A", c + 1))
    NI = len(items)
    assert NI % 2 == 0
    item_at = {it: n for n, it in enumerate(items)}

    with ExitStack() as ctx:
        def sb(name, shape, dt=F32):
            return ctx.enter_context(nc.sbuf_tensor(name, shape, dt))

        def bank(name):
            return ctx.enter_context(nc.psum_tensor(name, [P, 512], F32))

        def sem(name):
            return ctx.enter_context(nc.semaphore(name))

        ident = sb("ident", [P, P])
        ident_bf = sb("ident_bf", [P, P], BF16)
        wrap = sb("wrap", [KR, 2 * NF], BF16)
        select = sb("select", [KR, CHUNKS, SHIFTS, NF], BF16)
        replicate = sb("replicate", [KR, SHIFTS, NF], BF16)
        part_no = sb("part_no", [P, 1], I32)
        odd_bit = sb("odd_bit", [P, 1], I32)
        mask = sb("mask", [P, 2])
        w0_raw = sb("w0_raw", [H, NF, NF])
        w0_cols = sb("w0_cols", [H, NF, 2 * NF])
        w0_rows = sb("w0_rows", [H, 2 * NF, NF])
        w0_pairs = sb("w0_pairs", [H, NSHIFT, NF])
        w0_t = sb("w0_t", [KR, CHUNKS, H])
        w1_raw = sb("w1_raw", [H, NF, H])
        w1_t = sb("w1_t", [P, NF, H])
        wt1 = sb("wt1", [P, 2, M1])
        wt1_dense = sb("wt1_dense", [ND, M1])
        wt2 = sb("wt2", [P, M1 // P, M2])
        wt3 = sb("wt3", [P, M2 // P])
        bt1 = sb("bt1", [P, M1 // P])
        bt2 = sb("bt2", [P, M2 // P])
        dense_in = sb("dense_in", [P, TILES, ND])
        dense_t = sb("dense_t", [ND, NB])
        idx = [sb(f"idx{p}", [P, NF], I32) for p in range(2)]
        emb = [sb(f"emb{p}", [P, NF, D]) for p in range(2)]
        begun = sb("begun", [1, 1])
        rest = sb("rest", [P, D, NF])
        split = sb("split", [P, D, PARTS, NF], BF16)
        x3 = sb("x3", [KR, P, D], BF16)
        xa = sb("xa", [KR, P, D])
        prod = sb("prod", [KR, RING, COL])
        h1 = sb("h1", [H, P, D])
        h1_t = sb("h1_t", [P, GROUPS, H])
        xd = sb("xd", [P, GROUPS, 2, GF])
        g_sb = sb("g_sb", [H, GF, P])
        z2 = sb("z2", [H, P])
        m1 = sb("m1", [P, M1 // P, P])
        m2 = sb("m2", [P, M2 // P, P])
        y = sb("y", [1, NB])

        b_ex = [bank(f"b_ex{i}") for i in range(2)]
        b_h = bank("b_h")
        b_m = bank("b_m")
        b_g = [bank(f"b_g{i}") for i in range(4)]

        s_ids = [sem(f"ids_loaded{p}") for p in range(2)]
        s_gather = [sem(f"gathered{p}") for p in range(2)]
        s_begun = sem("gather_begun")
        s_w0 = sem("w0_loaded")
        s_w1 = sem("w1_loaded")
        s_dense = sem("dense_loaded")
        s_mlpw = sem("mlp_weights_loaded")
        s_zero = sem("pool_zeroed")
        s_const = sem("pool_consts")
        s_sel = sem("select_ready")
        s_mask = sem("mask_ready")
        s_w0v = sem("w0_pairs_step")
        s_prep = sem("prep_transposed")
        s_prepped = sem("prep_copied")
        s_split = sem("split_step")
        s_t3 = sem("parts_transposed")
        s_x3 = sem("x3_ready")
        s_ex = sem("expanded")
        s_xa = sem("xa_ready")
        s_prod = sem("product_ready")
        s_l1 = sem("product_used")
        s_h1 = sem("h1_ready")
        s_ht = sem("h1_transposed")
        s_htc = sem("h1_t_ready")
        s_xt = sem("x_transposed")
        s_xd = sem("xd_ready")
        s_g = sem("g_done")
        s_gc = sem("g_ready")
        s_l2 = sem("layer2_done")
        s_z2 = sem("z2_ready")
        s_m1 = sem("mlp1_done")
        s_m1c = sem("m1_ready")
        s_m2 = sem("mlp2_done")
        s_m2c = sem("m2_ready")
        s_m3 = sem("mlp3_done")
        s_y = sem("y_ready")
        s_out = sem("out_stored")

        block = ctx.enter_context(nc.Block())

        prep = [("w0", 0, 4), ("w0", 4, CHUNKS - 5), ("w0", CHUNKS - 1, 1), ("dense", 0, 4), ("dense", 4, 4)]
        prep += [("w1", f, min(4, NF - f)) for f in range(0, NF, 4)]

        def over_tiles(eng, tile, last):
            tile(0, 0, False, False)
            tile(1, 1, True, False)
            with eng.Fori(1, TILES // 2) as u:
                tile(2 * u, 0, True, True)
                tile(2 * u + 1, 1, True, True)
            last()

        @block.sync
        def _(sp):
            def load_ids(t, par, has1, has2):
                if has2:
                    sp.wait_ge(s_gather[par], (t - par) * (8 * NF))
                sp.dma_start(idx[par][:, :], ids[bass.ds(t * P, P), :]).then_inc(s_ids[par], 16)

            load_ids(0, 0, False, False)
            sp.dma_start(w0_raw[:, :, :], w0.rearrange("h (f q) o -> h f (q o)", f=NF)).then_inc(s_w0, 16)
            load_ids(1, 1, True, False)
            sp.dma_start(dense_in[:, :, :], dense.rearrange("(t p) n -> p t n", p=P)).then_inc(s_dense, 16)
            sp.dma_start(w1_raw[:, :, :], w1.rearrange("h (f q) o -> h f (q o)", f=NF)).then_inc(s_w1, 16)
            sp.dma_start(wt1[:, :, :], w_top1[0:2 * P, :].rearrange("(k p) n -> p k n", p=P)).then_inc(s_mlpw, 16)
            sp.dma_start(wt1_dense[:, :], w_top1[2 * P:2 * P + ND, :]).then_inc(s_mlpw, 16)
            sp.dma_start(wt2[:, :, :], w_top2.rearrange("(k p) n -> p k n", p=P)).then_inc(s_mlpw, 16)
            with nc.allow_non_contiguous_dma(reason="biases and the last layer, 1024 numbers, one per partition"):
                sp.dma_start(bt1[:, :], b_top1.rearrange("(k p) -> p k", p=P)).then_inc(s_mlpw, 16)
                sp.dma_start(bt2[:, :], b_top2.rearrange("(k p) -> p k", p=P)).then_inc(s_mlpw, 16)
                sp.dma_start(wt3[:, :], w_top3.rearrange("(k p) n -> p (k n)", p=P)).then_inc(s_mlpw, 16)
            with sp.Fori(1, TILES // 2) as u:
                load_ids(2 * u, 0, True, True)
                load_ids(2 * u + 1, 1, True, True)
            sp.wait_ge(s_y, TILES)
            sp.dma_start(out.rearrange("n o -> o n"), y[:, :]).then_inc(s_out, 16)
            sp.wait_ge(s_out, 16)

        @block.gpsimd
        def _(pool):
            pool.memset(ident[:, :], 0.0).then_inc(s_zero, 1)
            pool.memset(wrap[:, :], 0.0).then_inc(s_zero, 1)
            pool.iota(part_no[:, :], pattern=[[0, 1]], base=0, channel_multiplier=1).then_inc(s_const, 1)
            pool.wait_ge(s_zero, 2)
            pool.affine_select(out=ident[:, :], in_=ident[:, :], compare_op=ALU.not_equal, fill=1.0, base=0,
                               pattern=[[-1, P]], channel_multiplier=1).then_inc(s_const, 1)
            for n, m in enumerate((-1, 0, 1, 2)):
                if n:
                    pool.wait_ge(s_const, n + 2)
                pool.affine_select(out=wrap[:, :], in_=wrap[:, :], compare_op=ALU.not_equal, fill=1.0,
                                   base=-NF * m, pattern=[[-1, 2 * NF]], channel_multiplier=1).then_inc(s_const, 1)

            def gather(t, par, has1, has2):
                if has2:
                    pool.wait_ge(s_split, 4 * t - 4)
                pool.wait_ge(s_ids[par], (t - par) * 8 + 16)
                if has1:
                    pool.wait_ge(s_begun, t)
                pool.tensor_tensor(begun[:, :], ident[0:1, 0:1], ident[0:1, 0:1], ALU.add).then_inc(s_begun, 1)
                for f in range(NF):
                    pool.indirect_dma_start(emb[par][:, f, :], None, tables[f],
                                            bass.IndirectOffsetOnAxis(ap=idx[par][:, f:f + 1], axis=0)
                                            ).then_inc(s_gather[par], 16)

            over_tiles(pool, gather, lambda: None)

        @block.vector
        def _(dve):
            dve.wait_ge(s_const, 6)
            dve.tensor_copy(ident_bf[:, :], ident[:, :]).then_inc(s_sel, 1)
            for j in range(CHUNKS):
                for s in range(SHIFTS):
                    k = SHIFTS * j + s
                    if k <= NF:
                        dve.tensor_copy(select[:, j, s, :], wrap[:, k:k + NF]).then_inc(s_sel, 1)
            for s in range(SHIFTS):
                dve.tensor_copy(replicate[:, s, :], wrap[:, 0:NF]).then_inc(s_sel, 1)
            dve.tensor_single_scalar(odd_bit[:, :], part_no[:, :], D, op=ALU.bitwise_and).then_inc(s_mask, 1)
            dve.wait_ge(s_mask, 1)
            dve.tensor_single_scalar(mask[:, 0:1], odd_bit[:, :], 0, op=ALU.is_equal).then_inc(s_mask, 1)
            dve.tensor_single_scalar(mask[:, 1:2], odd_bit[:, :], D, op=ALU.is_equal).then_inc(s_mask, 1)
            dve.wait_ge(s_mask, 3)
            for c in range(2):
                dve.tensor_copy(xd[:, :, c, NF], mask[:, c:c + 1].broadcast_to([P, GROUPS])).then_inc(s_mask, 1)
            dve.wait_ge(s_w0, 16)
            dve.tensor_copy(w0_cols[:, :, 0:NF], w0_raw[:, :, :]).then_inc(s_w0v, 1)
            dve.tensor_copy(w0_cols[:, :, NF:2 * NF], w0_raw[:, :, :]).then_inc(s_w0v, 1)
            dve.tensor_copy(w0_rows[:, 0:NF, :], w0_raw[:, :, :]).then_inc(s_w0v, 1)
            dve.tensor_copy(w0_rows[:, NF:2 * NF, :], w0_raw[:, :, :]).then_inc(s_w0v, 1)
            dve.wait_ge(s_w0v, 4)
            fc = w0_cols[:, :, :].rearrange("h f q -> h (f q)")
            fr = w0_rows[:, :, :].rearrange("h f q -> h (f q)")
            dve.tensor_copy(w0_pairs[:, 0, :], fc[:, 0:(2 * NF + 1) * (NF - 1) + 1:2 * NF + 1]).then_inc(s_w0v, 1)
            for k in range(1, NSHIFT):
                a = fc[:, k:k + (2 * NF + 1) * (NF - 1) + 1:2 * NF + 1]
                b = fr[:, NF * k:NF * k + (NF + 1) * (NF - 1) + 1:NF + 1]
                dve.tensor_tensor(w0_pairs[:, k, :], a, b, ALU.add).then_inc(s_w0v, 1)

            def split_parts(t, par, has1):
                x = emb[par][:, :, :].rearrange("p f d -> p d f")
                dve.wait_ge(s_gather[par], (t - par) * (8 * NF) + 16 * NF)
                if has1:
                    dve.wait_ge(s_t3, 2 * t)
                dve.tensor_copy(split[:, :, 0, :], x).then_inc(s_split, 1)
                dve.wait_ge(s_split, 4 * t + 1)
                dve.tensor_tensor(rest[:, :, :], x, split[:, :, 0, :], ALU.subtract).then_inc(s_split, 1)
                dve.wait_ge(s_split, 4 * t + 2)
                dve.tensor_copy(split[:, :, 1, :], rest[:, :, :]).then_inc(s_split, 1)
                dve.wait_ge(s_split, 4 * t + 3)
                dve.tensor_tensor(split[:, :, 2, :], rest[:, :, :], split[:, :, 1, :], ALU.subtract).then_inc(s_split, 1)

            def mlp2_out(t):
                dve.wait_ge(s_m2, t + 1)
                for k in range(M2 // P):
                    i = dve.tensor_scalar(m2[:, k, :], b_m[:, k * P:(k + 1) * P], bt2[:, k:k + 1], 0.0, ALU.add, ALU.max)
                i.then_inc(s_m2c, 1)

            def mlp3_out(t):
                dve.wait_ge(s_m3, t + 1)
                dve.tensor_copy(y[:, bass.ds(t * P, P)], b_m[0:1, 0:P]).then_inc(s_y, 1)

            def products(t, c, has1):
                for j in range(CHUNKS):
                    n, it = c * CHUNKS + j, item_at[("B", c, j)]
                    if j == 0:
                        dve.wait_ge(s_xa, BLOCKS * t + c + 1)
                    dve.wait_ge(s_ex, NI * t + it + 1)
                    if has1 or n >= RING:
                        dve.wait_ge(s_l1, PT * t + n - RING + 1)
                    K = rows[j]
                    dve.tensor_tensor(prod[0:K, n % RING, :], xa[0:K, c * SB:(c + 1) * SB, :].rearrange("k b d -> k (b d)"),
                                      b_ex[it % 2][0:K, :], ALU.mult).then_inc(s_prod, 1)

            def spread_x(t, has1):
                for k in range(2):
                    dve.wait_ge(s_xt, 2 * t + k + 1)
                    src = b_g[2 + k][:, 0:8 * NF].rearrange("p (g f) -> p g f", f=NF)
                    for c in range(2):
                        i = dve.tensor_scalar(xd[:, 8 * k:8 * k + 8, c, 0:NF], src, mask[:, c:c + 1], None, ALU.mult)
                    i.then_inc(s_xd, 1)

            def tile(t, par, has1, has2, more=True):
                products(t, 0, has1)
                if has2:
                    mlp2_out(t - 2)
                products(t, 1, has1)
                if has2:
                    mlp3_out(t - 2)
                products(t, 2, has1)
                products(t, 3, has1)
                if more:
                    split_parts(t + 1, 1 - par, True)
                spread_x(t, has1)

            split_parts(0, 0, False)
            tile(0, 0, False, False)
            tile(1, 1, True, False)
            with dve.Fori(1, TILES // 2 - 1) as u:
                tile(2 * u, 0, True, True)
                tile(2 * u + 1, 1, True, True)
            tile(TILES - 2, 0, True, True)
            tile(TILES - 1, 1, True, True, more=False)
            for t in (TILES - 2, TILES - 1):
                mlp2_out(t)
                mlp3_out(t)

        @block.scalar
        def _(act):
            for k, (kind, a, n) in enumerate(prep):
                act.wait_ge(s_prep, k + 1)
                if kind == "w0":
                    act.activation(w0_t[0:rows[a], a:a + n, :], b_g[k % 4][0:rows[a], 0:n * P].rearrange("p (j h) -> p j h", h=P),
                                   ACT.Copy).then_inc(s_prepped, 1)
                elif kind == "dense":
                    act.activation(dense_t[:, a * P:(a + n) * P], b_g[k % 4][0:ND, 0:n * P], ACT.Copy).then_inc(s_prepped, 1)
                else:
                    act.activation(w1_t[:, a:a + n, :], b_g[k % 4][:, 0:n * P].rearrange("p (j h) -> p j h", h=P),
                                   ACT.Copy).then_inc(s_prepped, 1)
            act.wait_ge(s_mlpw, 96)

            def copy_x3(t, has1):
                for k in range(2):
                    act.wait_ge(s_t3, 2 * t + k + 1)
                    act.activation(x3[:, :, 8 * k:8 * k + 8].rearrange("p b d -> p d b"), b_g[k][0:KR, :].bitcast(BF16).rearrange("p (d b) -> p d b", b=P),
                                   ACT.Copy).then_inc(s_x3, 1)

            def copy_xa(t, c, has1):
                act.wait_ge(s_ex, NI * t + item_at[("A", c)] + 1)
                if has1:
                    act.wait_ge(s_prod, PT * t)
                act.activation(xa[:, c * SB:(c + 1) * SB, :], b_ex[item_at[("A", c)] % 2][0:KR, :].rearrange("p (b d) -> p b d", d=D),
                               ACT.Copy).then_inc(s_xa, 1)

            def copy_h1(t, c):
                act.wait_ge(s_l1, PT * t + CHUNKS * (c + 1))
                act.activation(h1[:, c * SB:(c + 1) * SB, :], b_h[:, :].rearrange("p (b d) -> p b d", d=D),
                               ACT.Copy).then_inc(s_h1, 1)

            def copy_h1_t(t, k):
                act.wait_ge(s_ht, 4 * t + k + 1)
                act.activation(h1_t[:, 4 * k:4 * k + 4, :], b_g[(2 + k) % 4][:, :].rearrange("p (g h) -> p g h", h=H),
                               ACT.Copy).then_inc(s_htc, 1)

            def copy_g(t, b):
                g0, n = sum(BATCHES[:b]), BATCHES[b]
                act.wait_ge(s_g, 3 * t + b + 1)
                for s in range(4):
                    dst = g_sb[:, :, :].rearrange("q f (g s c) -> q g s c f", s=4, c=2)[:, g0:g0 + n, s]
                    src = b_g[s][:, 0:n * 2 * GF].rearrange("q (g c f) -> q g c f", c=2, f=GF)
                    act.activation(dst, src, ACT.Copy).then_inc(s_gc, 1)

            def mlp1_out(t):
                act.wait_ge(s_m1, t + 1)
                for k in range(M1 // P):
                    i = act.activation(m1[:, k, :], b_m[:, k * P:(k + 1) * P], ACT.Relu, bias=bt1[:, k:k + 1])
                i.then_inc(s_m1c, 1)

            def copy_z2(t):
                act.wait_ge(s_l2, t + 1)
                act.activation(z2[:, :], b_m[:, 0:P], ACT.Copy).then_inc(s_z2, 1)

            def tile(t, par, has1, has2):
                copy_x3(t, has1)
                if has2:
                    mlp1_out(t - 2)
                if has1:
                    copy_h1_t(t - 1, 0)
                    copy_h1_t(t - 1, 1)
                copy_xa(t, 0, has1)
                if has1:
                    copy_h1_t(t - 1, 2)
                    copy_h1_t(t - 1, 3)
                for c in range(BLOCKS - 1):
                    copy_xa(t, c + 1, has1)
                    copy_h1(t, c)
                    if has1:
                        copy_g(t - 1, c)
                if has1:
                    copy_z2(t - 1)
                copy_h1(t, BLOCKS - 1)

            def tail():
                t = TILES - 1
                mlp1_out(t - 1)
                for k in range(4):
                    copy_h1_t(t, k)
                for b in range(3):
                    copy_g(t, b)
                copy_z2(t)
                mlp1_out(t)

            over_tiles(act, tile, tail)

        @block.tensor
        def _(pe):
            pe.wait_ge(s_const, 2)
            for k, (kind, a, n) in enumerate(prep):
                if k >= 4:
                    pe.wait_ge(s_prepped, k - 3)
                if kind == "w0":
                    pe.wait_ge(s_w0v, 4 + NSHIFT)
                if kind == "dense":
                    pe.wait_ge(s_dense, 16)
                if kind == "w1":
                    pe.wait_ge(s_w1, 16)
                for i in range(n):
                    dst = b_g[k % 4][:, i * P:(i + 1) * P]
                    if kind == "w0":
                        r = rows[a + i]
                        m = pe.transpose(dst[0:r, :], w0_pairs[:, :, :].rearrange("h k f -> h (k f)")[:, (a + i) * KR:(a + i) * KR + r], ident[:, :])
                    elif kind == "dense":
                        m = pe.transpose(dst[0:ND, :], dense_in[:, a + i, :], ident[:, :])
                    else:
                        m = pe.transpose(dst, w1_raw[:, a + i, :], ident[:, :])
                m.then_inc(s_prep, 1)
            pe.wait_ge(s_sel, 1 + CHUNKS * SHIFTS + SHIFTS)
            pe.wait_ge(s_prepped, len(prep))
            pe.wait_ge(s_mlpw, 96)
            pe.wait_ge(s_mask, 5)

            def transpose_parts(t, has1, has2):
                pe.wait_ge(s_split, 4 * t + 4)
                if has2:
                    pe.wait_ge(s_gc, 12 * (t - 1))
                elif has1:
                    pass
                for k in range(2):
                    for i in range(8):
                        dst = b_g[k][0:KR, :].bitcast(BF16)[:, i * P:(i + 1) * P]
                        m = pe.transpose(dst, split[:, 8 * k + i, :, :].rearrange("p a f -> p (a f)"), ident_bf[:, :])
                    m.then_inc(s_t3, 1)

            def transpose_h1(t, k):
                for i in range(4):
                    g = 4 * k + i
                    src = h1[:, 8 * g:8 * g + 8, :].rearrange("q b d -> q (b d)")
                    m = pe.transpose(b_g[(2 + k) % 4][:, i * P:(i + 1) * P], src, ident[:, :])
                m.then_inc(s_ht, 1)

            def expand(t, n, has1):
                it = items[n]
                if n < 2:
                    if n == 0:
                        pe.wait_ge(s_x3, 2 * t + 2)
                    if has1:
                        pe.wait_ge(s_prod, PT * t)
                else:
                    old = items[n - 2]
                    if old[0] == "A":
                        pe.wait_ge(s_xa, BLOCKS * t + old[1] + 1)
                    else:
                        pe.wait_ge(s_prod, PT * t + old[1] * CHUNKS + old[2] + 1)
                c = it[1]
                w = replicate[:, :, :] if it[0] == "A" else select[:, it[2], :, :]
                K = KR if it[0] == "A" else rows[it[2]]
                pe.matmul(b_ex[n % 2][0:K, :], w.rearrange("p s f -> p (s f)")[:, 0:K],
                          x3[:, c * SB:(c + 1) * SB, :].rearrange("p b d -> p (b d)"),
                          start=True, stop=True).then_inc(s_ex, 1)

            def layer1(t, c, j, has1):
                n = c * CHUNKS + j
                if j == 0 and (has1 or c):
                    pe.wait_ge(s_h1, BLOCKS * t + c)
                pe.wait_ge(s_prod, PT * t + n + 1)
                K = rows[j]
                pe.matmul(b_h[:, :], w0_t[0:K, j, :], prod[0:K, n % RING, :],
                          start=(j == 0), stop=(j == CHUNKS - 1)).then_inc(s_l1, 1)

            def contract_d(t, b):
                if b == 0:
                    pe.wait_ge(s_htc, 4 * t + 4)
                    pe.wait_ge(s_xd, 2 * t + 2)
                else:
                    pe.wait_ge(s_gc, 12 * t + 4 * b)
                g0 = sum(BATCHES[:b])
                for g in range(BATCHES[b]):
                    for s in range(4):
                        r = slice(32 * s, 32 * s + 32)
                        m = pe.matmul(b_g[s][:, g * 2 * GF:(g + 1) * 2 * GF], h1_t[r, g0 + g, :],
                                      xd[r, g0 + g, :, :].rearrange("p c f -> p (c f)"), start=True, stop=True)
                m.then_inc(s_g, 1)

            def layer2(t, first):
                pe.wait_ge(s_gc, 12 * t + 12)
                if not first:
                    pe.wait_ge(s_y, t)
                for f in range(NF):
                    m = pe.matmul(b_m[:, 0:P], w1_t[:, f, :], g_sb[:, f, :], start=(f == 0), stop=(f == NF - 1))
                m.then_inc(s_l2, 1)

            def mlp1(t):
                pe.wait_ge(s_z2, t + 1)
                for k in range(M1 // P):
                    o, cols = b_m[:, k * P:(k + 1) * P], slice(k * P, (k + 1) * P)
                    pe.matmul(o, wt1[:, 0, cols], g_sb[:, NF, :], start=True, stop=False)
                    pe.matmul(o, wt1[:, 1, cols], z2[:, :], start=False, stop=False)
                    m = pe.matmul(o, wt1_dense[:, cols], dense_t[:, bass.ds(t * P, P)], start=False, stop=True)
                m.then_inc(s_m1, 1)

            def mlp2(t):
                pe.wait_ge(s_m1c, t + 1)
                for k in range(M2 // P):
                    for i in range(M1 // P):
                        m = pe.matmul(b_m[:, k * P:(k + 1) * P], wt2[:, i, k * P:(k + 1) * P], m1[:, i, :],
                                      start=(i == 0), stop=(i == M1 // P - 1))
                m.then_inc(s_m2, 1)

            def mlp3(t):
                pe.wait_ge(s_m2c, t + 1)
                for i in range(M2 // P):
                    m = pe.matmul(b_m[0:1, 0:P], wt3[:, i:i + 1], m2[:, i, :], start=(i == 0), stop=(i == M2 // P - 1))
                m.then_inc(s_m3, 1)

            def transpose_x(t):
                for k in range(2):
                    for i in range(8):
                        g = 8 * k + i
                        src = xa[0:NF, 8 * g:8 * g + 8, :].rearrange("f b d -> f (b d)")
                        m = pe.transpose(b_g[2 + k][:, i * NF:(i + 1) * NF], src, ident[0:NF, 0:NF])
                    m.then_inc(s_xt, 1)

            def tile(t, par, has1, has2):
                transpose_parts(t, has1, has2)
                if has2:
                    mlp1(t - 2)
                if has1:
                    pe.wait_ge(s_h1, BLOCKS * t)
                    pe.wait_ge(s_xd, 2 * t)
                    transpose_h1(t - 1, 0)
                    transpose_h1(t - 1, 1)
                for n in range(2):
                    expand(t, n, has1)
                if has1:
                    transpose_h1(t - 1, 2)
                    transpose_h1(t - 1, 3)
                for n in range(2, NI + 2):
                    if n < NI:
                        expand(t, n, has1)
                    if n == NI and has1:
                        layer2(t - 1, not has2)
                    done = items[n - 2]
                    if done[0] == "B":
                        _, c, j = done
                        layer1(t, c, j, has1)
                        if j == CHUNKS - 1 and c < BLOCKS - 1:
                            if has2 and c == 0:
                                mlp2(t - 2)
                            if has2 and c == 1:
                                mlp3(t - 2)
                            if has1:
                                contract_d(t - 1, c)
                transpose_x(t)

            def tail():
                t = TILES - 1
                mlp1(t - 1)
                pe.wait_ge(s_h1, BLOCKS * (t + 1))
                pe.wait_ge(s_xd, 2 * t + 2)
                for k in range(4):
                    transpose_h1(t, k)
                mlp2(t - 1)
                contract_d(t, 0)
                mlp3(t - 1)
                contract_d(t, 1)
                contract_d(t, 2)
                layer2(t, False)
                mlp1(t)
                mlp2(t)
                mlp3(t)

            over_tiles(pe, tile, tail)


TABLES = [f"tbl_{f}" for f in range(39)]
_INS = ["dense_ctx", "ids"] + TABLES + ["W_top1", "b_top1", "W_top2", "b_top2", "W_top3", "L0_rec_W0", "L0_rec_W1"]


def kernel(**inputs):
    import numpy as _np
    import concourse.bacc as _bacc
    from concourse import mybir as _mybir
    from concourse.bass_utils import run_bass_kernel_spmd as _run

    nc = _bacc.Bacc("TRN2", target_bir_lowering=False, num_devices=1)
    arrays, a = {}, {}
    for name in _INS:
        x = _np.ascontiguousarray(inputs[name])
        arrays[f"in_{name}"] = x
        a[name] = nc.dram_tensor(f"in_{name}", x.shape, _mybir.dt.from_np(x.dtype), kind="ExternalInput").ap()
    n = inputs["ids"].shape[0]
    out = nc.dram_tensor("out_y", (n, 1), _mybir.dt.float32, kind="ExternalOutput").ap()
    build(nc, a["dense_ctx"], a["ids"], [a[t] for t in TABLES], a["W_top1"], a["b_top1"], a["W_top2"], a["b_top2"],
          a["W_top3"], a["L0_rec_W0"], a["L0_rec_W1"], out)
    r = _run(nc, [arrays], core_ids=[0])
    return r.results[0]["out_y"]
```

```python
from contextlib import ExitStack

import concourse.bass as bass
from concourse import mybir

F32 = mybir.dt.float32
F32R = mybir.dt.float32r
I32 = mybir.dt.int32
ALU = mybir.AluOpType
ACT = mybir.ActivationFunctionType

P = 128
SHIFTS = 3
LAG = 2
PROD_RING = 3
PART_RING = 3
EARLY = 1
TRIPLE_AT = 11
SLOTS = 4
BANKLESS = ("L1", "L2+", "m3")
STEPS = [("m1", 0), ("L1", 0), ("XT", 0), ("L1", 1)] + [("HT", k) for k in range(4)]
STEPS += [("L1", 2), ("m2", 0), ("L1", 3), ("m3", 0), ("XT", 1), ("G", 0), ("G", 1), ("L1", 4), ("G", 2), ("G", 3)]
STEPS += [("L1", 5), ("XT", 2), ("G", 4), ("G", 5), ("L1", 6), ("G", 6), ("G", 7), ("L1", 7), ("XT", 3)]
STEPS += [("G", 8), ("G", 9), ("L1", 8), ("G", 10), ("G", 11), ("L1", 9)] + [("T", k) for k in range(4)]
STEPS += [("L1", 10), ("L2", 0), ("L1", 11), ("L2+", 1), ("L1", 12), ("L2+", 2), ("L2+", 3), ("L1", 13)]
BATCHES = (3, 3, 3, 3, 2, 2)


def build(nc, dense, ids, tables, w_top1, b_top1, w_top2, b_top2, w_top3, w0, w1, out):
    NB, NF = ids.shape
    D = tables[0].shape[1]
    H = w0.shape[0]
    ND = dense.shape[1]
    M1, M2 = w_top2.shape
    TILES = NB // P
    KR = SHIFTS * NF
    NSHIFT = NF // 2 + 1
    CHUNKS = -(-NSHIFT // SHIFTS)
    shifts = [min(SHIFTS, NSHIFT - SHIFTS * j) for j in range(CHUNKS)]
    rows = [n * NF for n in shifts]
    COL = 512
    SB = COL // D
    BLOCKS = P // SB
    HALF = 2 * COL
    NP = 2 * CHUNKS
    GROUPS = P // 8
    L2_PART = -(-NF // 4)
    GF = NF + 1
    assert NF % 2 == 1 and D == 16 and H == P and TILES % 2 == 0 and TILES >= 6

    steps = STEPS
    TILE_OF = {"T": 1, "XT": 0, "L1": 0, "HT": -1, "G": -1, "L2": -1, "L2+": -1, "m1": -2, "m2": -2, "m3": -2}
    PER = {"T": 4, "XT": 4, "HT": 4, "G": 12, "L2": 1, "m1": 1, "m2": 1}
    jobs = [s for s in steps if s[0] not in BANKLESS]
    bank_of = {job: n % 4 for n, job in enumerate(jobs)}
    tail_steps = [("m1", -1)] + [("HT", k) for k in range(4)] + [("m2", -1)]
    tail_steps += [("G", 0), ("G", 1), ("m3", -1)] + [("G", i) for i in range(2, 12)]
    tail_steps += [("L2", 0), ("L2+", 1), ("L2+", 2), ("L2+", 3), ("m1", 0), ("m2", 0), ("m3", 0)]
    tail_bank, turn = {}, 0
    for name, i in tail_steps:
        tail_bank[name, i] = turn % 4
        turn += name not in BANKLESS

    def own_bank(name, i, banks):
        return banks[{"m3": "m2", "L2+": "L2"}.get(name, name), 0 if name == "L2+" else i]

    def present(name, has1, has2, more):
        off = TILE_OF[name]
        return more if off == 1 else off == 0 or (has1 if off == -1 else has2)

    with ExitStack() as ctx:
        def sb(name, shape, dt=F32):
            return ctx.enter_context(nc.sbuf_tensor(name, shape, dt))

        def bank(name):
            return ctx.enter_context(nc.psum_tensor(name, [P, 512], F32))

        def sem(name):
            return ctx.enter_context(nc.semaphore(name))

        ident = sb("ident", [P, P])
        begun = sb("begun", [1, 1])
        part_no = sb("part_no", [P, 1], I32)
        strip_bits = sb("strip_bits", [P, 1], I32)
        mask = sb("mask", [P, 4])
        w0_hi = sb("w0_hi", [KR, CHUNKS, H], F32R)
        w0_lo = sb("w0_lo", [KR, CHUNKS, H], F32R)
        w1_t = sb("w1_t", [P, NF, H])
        wt1 = sb("wt1", [P, 2, M1])
        wt1_dense = sb("wt1_dense", [ND, M1])
        wt2 = sb("wt2", [P, M1 // P, M2])
        wt3 = sb("wt3", [P, M2 // P])
        bt1 = sb("bt1", [P, M1 // P])
        bt2 = sb("bt2", [P, M2 // P])
        dense_in = sb("dense_in", [P, TILES, ND])
        dense_t = sb("dense_t", [ND, NB])
        idx = [sb(f"idx{p}", [P, NF], I32) for p in range(2)]
        emb = [sb(f"emb{p}", [P, KR, D]) for p in range(2)]
        xa = [sb(f"xa{p}", [KR, P, D]) for p in range(2)]
        shifted = sb("shifted", [P, SLOTS, P * D])
        prod = sb("prod", [P, PROD_RING, HALF])
        p_hi = sb("p_hi", [KR, PART_RING, HALF], F32R)
        p_lo = sb("p_lo", [KR, PART_RING, HALF], F32R)
        h1 = sb("h1", [H, P, D])
        h1_t = sb("h1_t", [P, GROUPS, H])
        xd = [sb(f"xd{p}", [P, GROUPS, 4, GF]) for p in range(2)]
        g_sb = sb("g_sb", [H, GF, P])
        z2 = sb("z2", [H, P])
        m1 = sb("m1", [P, M1 // P, P])
        m2 = sb("m2", [P, M2 // P, P])
        y = sb("y", [1, NB])
        raw = shifted[:, :, :].rearrange("p s n -> p (s n)")
        w1_raw = raw[0:H, 0:NF * H].rearrange("h (f q) -> h f q", f=NF)
        w0_rows = prod[:, :, :].rearrange("h s n -> h (s n)")[:, 0:2 * NF * NF].rearrange("h (f q) -> h f q", q=NF)
        w0_pairs = h1[:, :, :].rearrange("h b d -> h (b d)")[:, 0:NSHIFT * NF].rearrange("h (k f) -> h k f", f=NF)
        w0_cols = raw[0:H, NF * H:NF * H + 2 * NF * NF].rearrange("h (f q) -> h f q", f=NF)

        b_h = [bank(f"b_h{i}") for i in range(BLOCKS)]
        b_r = [bank(f"b_r{i}") for i in range(4)]

        s_ids = [sem(f"ids_loaded{p}") for p in range(2)]
        s_gather = [sem(f"gathered{p}") for p in range(2)]
        s_begun = sem("gather_begun")
        s_w0 = sem("w0_loaded")
        s_w1 = sem("w1_loaded")
        s_dense = sem("dense_loaded")
        s_mlpw = sem("mlp_weights_loaded")
        s_zero = sem("pool_zeroed")
        s_const = sem("pool_consts")
        s_mask = sem("mask_ready")
        s_w0v = sem("w0_pairs_step")
        s_prep = sem("prep_transposed")
        s_prepped = sem("prep_copied")
        s_w0lo = sem("w0_lo_ready")
        s_emb3 = sem("emb_tripled")
        s_t = sem("emb_transposed")
        s_xa = sem("xa_ready")
        s_shift = [sem(f"shifted{k}") for k in range(SLOTS)]
        s_prod = sem("product_ready")
        s_hi = sem("hi_ready")
        s_lo = sem("lo_ready")
        s_l1 = sem("product_used")
        s_h1 = sem("h1_ready")
        s_ht = sem("h1_transposed")
        s_htc = sem("h1_t_ready")
        s_xt = sem("x_transposed")
        s_xd = sem("xd_ready")
        s_g = sem("g_done")
        s_gc = sem("g_ready")
        s_l2 = sem("layer2_done")
        s_z2 = sem("z2_ready")
        s_m1 = sem("mlp1_done")
        s_m1c = sem("m1_ready")
        s_m2 = sem("mlp2_done")
        s_m2c = sem("m2_ready")
        s_m3 = sem("mlp3_done")
        s_y = sem("y_ready")
        s_out = sem("out_stored")
        copied = {"T": s_xa, "XT": s_xd, "HT": s_htc, "G": s_gc, "L2": s_z2, "m1": s_m1c, "m2": s_y}

        block = ctx.enter_context(nc.Block())

        prep = [("w0", 0, 4), ("w0", 4, CHUNKS - 5), ("w0", CHUNKS - 1, 1), ("dense", 0, 4), ("dense", 4, 4)]
        prep += [("w1", f, min(4, NF - f)) for f in range(0, NF, 4)]
        W0_PREPS = 3

        def over_tiles(eng, tile, last):
            tile(0, 0, False, False, True)
            tile(1, 1, True, False, True)
            with eng.Fori(1, TILES // 2 - 1) as u:
                tile(2 * u, 0, True, True, True)
                tile(2 * u + 1, 1, True, True, True)
            tile(TILES - 2, 0, True, True, True)
            tile(TILES - 1, 1, True, True, False)
            last()

        def last_use(n, ring):
            return n - ring if n >= ring else n + (NP - 1 - n) // ring * ring - NP

        def slot_uses(j):
            same = [i for i in range(CHUNKS) if i % SLOTS == j % SLOTS]
            return sum(shifts[i] for i in same), sum(shifts[i] for i in same if i <= j)

        @block.sync
        def _(sp):
            def load_ids(t, par):
                sp.dma_start(idx[par][:, :], ids[bass.ds(t * P, P), :]).then_inc(s_ids[par], 16)

            load_ids(0, 0)
            sp.dma_start(w0_rows[:, 0:NF, :], w0.rearrange("h (f q) o -> h f (q o)", f=NF)).then_inc(s_w0, 16)
            load_ids(1, 1)
            sp.dma_start(dense_in[:, :, :], dense.rearrange("(t p) n -> p t n", p=P)).then_inc(s_dense, 16)
            sp.dma_start(w1_raw, w1.rearrange("h (f q) o -> h f (q o)", f=NF)).then_inc(s_w1, 16)
            sp.dma_start(wt1[:, :, :], w_top1[0:2 * P, :].rearrange("(k p) n -> p k n", p=P)).then_inc(s_mlpw, 16)
            sp.dma_start(wt1_dense[:, :], w_top1[2 * P:2 * P + ND, :]).then_inc(s_mlpw, 16)
            sp.dma_start(wt2[:, :, :], w_top2.rearrange("(k p) n -> p k n", p=P)).then_inc(s_mlpw, 16)
            with nc.allow_non_contiguous_dma(reason="biases and the last layer, 1024 numbers, one per partition"):
                sp.dma_start(bt1[:, :], b_top1.rearrange("(k p) -> p k", p=P)).then_inc(s_mlpw, 16)
                sp.dma_start(bt2[:, :], b_top2.rearrange("(k p) -> p k", p=P)).then_inc(s_mlpw, 16)
                sp.dma_start(wt3[:, :], w_top3.rearrange("(k p) n -> p (k n)", p=P)).then_inc(s_mlpw, 16)

            def tile(t, par, has1, has2, more):
                sp.wait_ge(s_xa, 4 * t + 4)
                if more and not (isinstance(t, int) and t >= TILES - 2):
                    sp.wait_ge(s_gather[par], (t - par) * (8 * NF) + 16 * NF)
                    load_ids(t + 2, par)
                for j in range(CHUNKS):
                    if has1 or j >= SLOTS:
                        last = 2 * (j - SLOTS) + 2 if j >= SLOTS else 2 * (j + (CHUNKS - 1 - j) // SLOTS * SLOTS) + 2 - NP
                        sp.wait_ge(s_prod, NP * t + last)
                    for s in range(shifts[j]):
                        k = SHIFTS * j + s
                        sp.dma_start(shifted[NF * s:NF * (s + 1), j % SLOTS, :],
                                     xa[par][k:k + NF, :, :].rearrange("f b d -> f (b d)")).then_inc(s_shift[j % SLOTS], 16)

            over_tiles(sp, tile, lambda: None)
            sp.wait_ge(s_y, TILES)
            sp.dma_start(out.rearrange("n o -> o n"), y[:, :]).then_inc(s_out, 16)
            sp.wait_ge(s_out, 16)

        @block.gpsimd
        def _(pool):
            pool.memset(ident[:, :], 0.0).then_inc(s_zero, 1)
            pool.iota(part_no[:, :], pattern=[[0, 1]], base=0, channel_multiplier=1).then_inc(s_const, 1)
            pool.wait_ge(s_zero, 1)
            pool.affine_select(out=ident[:, :], in_=ident[:, :], compare_op=ALU.not_equal, fill=1.0, base=0,
                               pattern=[[-1, P]], channel_multiplier=1).then_inc(s_const, 1)
            pool.wait_ge(s_const, 2)

            def gather(t, par, has1, has2, more):
                if has2:
                    pool.wait_ge(s_t, 4 * t - 4)
                if has1:
                    pool.wait_ge(s_begun, t)
                pool.wait_ge(s_ids[par], (t - par) * 8 + 16)
                pool.tensor_tensor(begun[:, :], ident[0:1, 0:1], ident[0:1, 0:1], ALU.add).then_inc(s_begun, 1)
                for f in range(NF):
                    pool.indirect_dma_start(emb[par][:, f, :], None, tables[f],
                                            bass.IndirectOffsetOnAxis(ap=idx[par][:, f:f + 1], axis=0)
                                            ).then_inc(s_gather[par], 16)

            over_tiles(pool, gather, lambda: None)

        @block.vector
        def _(dve):
            dve.wait_ge(s_const, 1)
            dve.tensor_single_scalar(strip_bits[:, :], part_no[:, :], 3 * D, op=ALU.bitwise_and).then_inc(s_mask, 1)
            dve.wait_ge(s_mask, 1)
            for c in range(4):
                dve.tensor_single_scalar(mask[:, c:c + 1], strip_bits[:, :], c * D, op=ALU.is_equal).then_inc(s_mask, 1)
            dve.wait_ge(s_mask, 5)
            for c in range(4):
                for p in range(2):
                    dve.tensor_copy(xd[p][:, :, c, NF], mask[:, c:c + 1].broadcast_to([P, GROUPS])).then_inc(s_mask, 1)
            dve.wait_ge(s_w0, 16)
            dve.tensor_copy(w0_cols[:, :, 0:NF], w0_rows[:, 0:NF, :]).then_inc(s_w0v, 1)
            dve.tensor_copy(w0_cols[:, :, NF:2 * NF], w0_rows[:, 0:NF, :]).then_inc(s_w0v, 1)
            dve.tensor_copy(w0_rows[:, NF:2 * NF, :], w0_rows[:, 0:NF, :]).then_inc(s_w0v, 1)
            dve.wait_ge(s_w0v, 3)
            fc = w0_cols.rearrange("h f q -> h (f q)")
            fr = w0_rows.rearrange("h f q -> h (f q)")
            dve.tensor_copy(w0_pairs[:, 0, :], fc[:, 0:(2 * NF + 1) * (NF - 1) + 1:2 * NF + 1]).then_inc(s_w0v, 1)
            for k in range(1, NSHIFT):
                a = fc[:, k:k + (2 * NF + 1) * (NF - 1) + 1:2 * NF + 1]
                b = fr[:, NF * k:NF * k + (NF + 1) * (NF - 1) + 1:NF + 1]
                dve.tensor_tensor(w0_pairs[:, k, :], a, b, ALU.add).then_inc(s_w0v, 1)
            for i in range(W0_PREPS):
                _, a, n = prep[i]
                dve.wait_ge(s_prepped, i + 1)
                dve.tensor_tensor(w0_lo[0:rows[a], a:a + n, :], b_r[i][0:rows[a], 0:n * P].rearrange("p (j h) -> p j h", h=P),
                                  w0_hi[0:rows[a], a:a + n, :].bitcast(F32), ALU.subtract).then_inc(s_w0lo, 1)

            def triple(t, par):
                dve.wait_ge(s_gather[par], (t - par) * (8 * NF) + 16 * NF)
                for s in range(1, SHIFTS):
                    i = dve.tensor_copy(emb[par][:, s * NF:(s + 1) * NF, :], emb[par][:, 0:NF, :])
                i.then_inc(s_emb3, 1)

            def multiply(t, par, n, has1):
                j, half = n // 2, n % 2
                if half == 0:
                    if j == 0:
                        dve.wait_ge(s_xa, 4 * t + 4)
                    total, upto = slot_uses(j)
                    dve.wait_ge(s_shift[j % SLOTS], 16 * total * t + 16 * upto)
                last = last_use(n, PROD_RING)
                if has1 or last >= 0:
                    dve.wait_ge(s_lo, NP * t + last + 1)
                K, cols = rows[j], slice(half * HALF, (half + 1) * HALF)
                dve.tensor_tensor(prod[0:K, n % PROD_RING, :], xa[par][0:K, :, :].rearrange("k b d -> k (b d)")[:, cols],
                                  shifted[0:K, j % SLOTS, cols], ALU.mult).then_inc(s_prod, 1)

            def lo_part(t, n, has1):
                dve.wait_ge(s_hi, NP * t + n + 1)
                if has1 or n >= PART_RING:
                    dve.wait_ge(s_l1, NP * t + last_use(n, PART_RING) + 1)
                K = rows[n // 2]
                dve.tensor_tensor(p_lo[0:K, n % PART_RING, :], prod[0:K, n % PROD_RING, :],
                                  p_hi[0:K, n % PART_RING, :].bitcast(F32), ALU.subtract).then_inc(s_lo, 1)

            def tile(t, par, has1, has2, more):
                for n in range(NP + LAG):
                    if n == TRIPLE_AT and more:
                        triple(t + 1, 1 - par)
                    if n < NP:
                        multiply(t, par, n, has1)
                    if n >= LAG:
                        lo_part(t, n - LAG, has1)

            triple(0, 0)
            over_tiles(dve, tile, lambda: None)

        @block.scalar
        def _(act):
            for k, (kind, a, n) in enumerate(prep):
                act.wait_ge(s_prep, k + 1)
                src = b_r[k % 4][:, 0:n * P]
                if kind == "w0":
                    act.activation(w0_hi[0:rows[a], a:a + n, :], src[0:rows[a], :].rearrange("p (j h) -> p j h", h=P),
                                   ACT.Copy).then_inc(s_prepped, 1)
                elif kind == "dense":
                    act.activation(dense_t[:, a * P:(a + n) * P], src[0:ND, :], ACT.Copy).then_inc(s_prepped, 1)
                else:
                    act.activation(w1_t[:, a:a + n, :], src.rearrange("p (j h) -> p j h", h=P),
                                   ACT.Copy).then_inc(s_prepped, 1)
            act.wait_ge(s_mlpw, 96)
            act.wait_ge(s_mask, 5)

            def copy_xa(t, par, k, has):
                act.wait_ge(s_t, 4 * t + k + 1)
                if has and k == 0:
                    act.wait_ge(s_prod, NP * (t - 1))
                src = b_r[bank_of["T", k]][0:KR, :].rearrange("p (d b) -> p d b", b=P)
                act.activation(xa[par][:, :, 4 * k:4 * k + 4].rearrange("p b d -> p d b"), src, ACT.Copy).then_inc(s_xa, 1)

            def hi_part(t, n, has1):
                act.wait_ge(s_prod, NP * t + n + 1)
                if has1 or n >= PART_RING:
                    act.wait_ge(s_l1, NP * t + last_use(n, PART_RING) + 1)
                K = rows[n // 2]
                act.activation(p_hi[0:K, n % PART_RING, :], prod[0:K, n % PROD_RING, :], ACT.Copy).then_inc(s_hi, 1)

            def copy_h1(t):
                for c in range(BLOCKS):
                    act.wait_ge(s_l1, NP * t + NP - 1 + c // 2)
                    act.activation(h1[:, c * SB:(c + 1) * SB, :], b_h[c][:, :].rearrange("p (b d) -> p b d", d=D),
                                   ACT.Copy).then_inc(s_h1, 1)

            def copy_h1_t(t, k, b):
                act.wait_ge(s_ht, 4 * t + k + 1)
                act.activation(h1_t[:, 4 * k:4 * k + 4, :], b_r[b][:, :].rearrange("p (g h) -> p g h", h=H),
                               ACT.Copy).then_inc(s_htc, 1)

            def spread_x(t, par, k, b):
                act.wait_ge(s_xt, 4 * t + k + 1)
                src = b_r[b][:, 0:4 * KR].rearrange("p (g f) -> p g f", f=KR)[:, :, 0:NF]
                for c in range(4):
                    i = act.activation(xd[par][:, 4 * k:4 * k + 4, c, 0:NF], src, ACT.Copy, scale=mask[:, c:c + 1])
                i.then_inc(s_xd, 1)

            def copy_g(t, i, b):
                batch, s = divmod(i, 2)
                g0, n = sum(BATCHES[:batch]), BATCHES[batch]
                act.wait_ge(s_g, 12 * t + i + 1)
                dst = g_sb[:, :, :].rearrange("q f (g s c) -> q g s c f", s=2, c=4)[:, g0:g0 + n, s]
                src = b_r[b][:, 0:n * 4 * GF].rearrange("q (g c f) -> q g c f", c=4, f=GF)
                act.activation(dst, src, ACT.Copy).then_inc(s_gc, 1)

            def mlp1_out(t, b):
                act.wait_ge(s_m1, t + 1)
                for k in range(M1 // P):
                    i = act.activation(m1[:, k, :], b_r[b][:, k * P:(k + 1) * P], ACT.Relu, bias=bt1[:, k:k + 1])
                i.then_inc(s_m1c, 1)

            def mlp2_out(t, b):
                act.wait_ge(s_m2, t + 1)
                for k in range(M2 // P):
                    i = act.activation(m2[:, k, :], b_r[b][:, k * P:(k + 1) * P], ACT.Relu, bias=bt2[:, k:k + 1])
                i.then_inc(s_m2c, 1)

            def mlp3_out(t, b):
                act.wait_ge(s_m3, t + 1)
                act.activation(y[:, bass.ds(t * P, P)], b_r[b][0:1, 0:P], ACT.Copy).then_inc(s_y, 1)

            def copy_z2(t, b):
                act.wait_ge(s_l2, t + 1)
                act.activation(z2[:, :], b_r[b][:, 0:P], ACT.Copy).then_inc(s_z2, 1)

            def copy_out(name, i, t, par, b, has):
                if name == "T":
                    copy_xa(t, par, i, has)
                elif name == "XT":
                    spread_x(t, par, i, b)
                elif name == "HT":
                    copy_h1_t(t, i, b)
                elif name == "G":
                    copy_g(t, i, b)
                elif name == "L2+" and i == 3:
                    copy_z2(t, b)
                elif name == "m1":
                    mlp1_out(t, b)
                elif name == "m2":
                    mlp2_out(t, b)
                elif name == "m3":
                    mlp3_out(t, b)

            def tile(t, par, has1, has2, more):
                done = -1
                parts = EARLY
                for name, i in steps:
                    if name == "L1":
                        done = i
                        continue
                    while parts < min(done + 1 + PART_RING, NP):
                        hi_part(t, parts, has1)
                        parts += 1
                    if not present(name, has1, has2, more):
                        continue
                    b = own_bank(name, i, bank_of)
                    copy_out(name, i, t + TILE_OF[name], par ^ (TILE_OF[name] & 1), b, has1)
                assert parts == NP
                if more:
                    for n in range(EARLY):
                        hi_part(t + 1, n, True)
                copy_h1(t)

            def tail():
                for name, i in tail_steps:
                    t = TILES - 1 + (i if name[0] == "m" else 0)
                    copy_out(name, i, t, 1, own_bank(name, i, tail_bank), True)

            for k in range(4):
                copy_xa(0, 0, k, False)
            for n in range(EARLY):
                hi_part(0, n, False)
            over_tiles(act, tile, tail)

        @block.tensor
        def _(pe):
            pe.wait_ge(s_const, 2)
            for k, (kind, a, n) in enumerate(prep):
                if k >= 4:
                    pe.wait_ge(s_prepped, k - 3)
                    if k - 4 < W0_PREPS:
                        pe.wait_ge(s_w0lo, k - 3)
                if kind == "w0":
                    pe.wait_ge(s_w0v, 3 + NSHIFT)
                if kind == "dense":
                    pe.wait_ge(s_dense, 16)
                if kind == "w1":
                    pe.wait_ge(s_w1, 16)
                for i in range(n):
                    dst = b_r[k % 4][:, i * P:(i + 1) * P]
                    if kind == "w0":
                        r = rows[a + i]
                        m = pe.transpose(dst[0:r, :], w0_pairs.rearrange("h k f -> h (k f)")[:, (a + i) * KR:(a + i) * KR + r], ident[:, :])
                    elif kind == "dense":
                        m = pe.transpose(dst[0:ND, :], dense_in[:, a + i, :], ident[:, :])
                    else:
                        m = pe.transpose(dst, w1_raw[:, a + i, :], ident[:, :])
                m.then_inc(s_prep, 1)
            pe.wait_ge(s_prepped, len(prep))
            pe.wait_ge(s_mlpw, 96)
            pe.wait_ge(s_mask, 13)

            def transpose_emb(t, par, k, b):
                if k == 0:
                    pe.wait_ge(s_emb3, t + 1)
                for i in range(4):
                    m = pe.transpose(b_r[b][0:KR, i * P:(i + 1) * P], emb[par][:, :, 4 * k + i], ident[:, :])
                m.then_inc(s_t, 1)

            def transpose_x(t, par, k, b):
                pe.wait_ge(s_xa, 4 * t + 4)
                for i in range(4):
                    g = 4 * k + i
                    m = pe.transpose(b_r[b][:, i * KR:(i + 1) * KR], xa[par][:, 8 * g:8 * g + 8, :].rearrange("f b d -> f (b d)"),
                                     ident[0:KR, 0:KR])
                m.then_inc(s_xt, 1)

            def transpose_h1(t, k, b):
                pe.wait_ge(s_h1, BLOCKS * t + k + 1)
                for i in range(4):
                    g = 4 * k + i
                    src = h1[:, 8 * g:8 * g + 8, :].rearrange("q b d -> q (b d)")
                    m = pe.transpose(b_r[b][:, i * P:(i + 1) * P], src, ident[:, :])
                m.then_inc(s_ht, 1)

            def layer1(t, n, has1):
                j, half = n // 2, n % 2
                if j == 0 and has1:
                    pe.wait_ge(s_h1, BLOCKS * t - BLOCKS + 2 * half + 2)
                pe.wait_ge(s_lo, NP * t + n + 1)
                K = rows[j]
                passes = [(w0_hi, p_hi), (w0_hi, p_lo), (w0_lo, p_hi)]
                for i, (w, p) in enumerate(passes):
                    for c in range(2):
                        m = pe.matmul(b_h[2 * half + c][:, :], w[0:K, j, :], p[0:K, n % PART_RING, c * COL:(c + 1) * COL],
                                      start=(j == 0 and i == 0), stop=(j == CHUNKS - 1 and i == 2))
                m.then_inc(s_l1, 1)

            def contract_d(t, par, i, banks):
                batch = i // 2
                if i == 0:
                    pe.wait_ge(s_htc, 4 * t + 4)
                    pe.wait_ge(s_xd, 4 * t + 4)
                g0 = sum(BATCHES[:batch])
                for g in range(BATCHES[batch]):
                    for s, b in enumerate(banks):
                        r = slice(64 * s, 64 * s + 64)
                        m = pe.matmul(b_r[b][:, g * 4 * GF:(g + 1) * 4 * GF], h1_t[r, g0 + g, :],
                                      xd[par][r, g0 + g, :, :].rearrange("p c f -> p (c f)"), start=True, stop=True)
                        if g == BATCHES[batch] - 1:
                            m.then_inc(s_g, 1)

            def layer2(t, part, b):
                if part == 0:
                    pe.wait_ge(s_gc, 12 * t + 12)
                for f in range(part * L2_PART, min(NF, (part + 1) * L2_PART)):
                    m = pe.matmul(b_r[b][:, 0:P], w1_t[:, f, :], g_sb[:, f, :], start=(f == 0), stop=(f == NF - 1))
                if part == 3:
                    m.then_inc(s_l2, 1)

            def mlp1(t, b):
                pe.wait_ge(s_z2, t + 1)
                for k in range(M1 // P):
                    o, cols = b_r[b][:, k * P:(k + 1) * P], slice(k * P, (k + 1) * P)
                    pe.matmul(o, wt1[:, 0, cols], g_sb[:, NF, :], start=True, stop=False)
                    pe.matmul(o, wt1[:, 1, cols], z2[:, :], start=False, stop=False)
                    m = pe.matmul(o, wt1_dense[:, cols], dense_t[:, bass.ds(t * P, P)], start=False, stop=True)
                m.then_inc(s_m1, 1)

            def mlp2(t, b):
                pe.wait_ge(s_m1c, t + 1)
                for k in range(M2 // P):
                    for i in range(M1 // P):
                        m = pe.matmul(b_r[b][:, k * P:(k + 1) * P], wt2[:, i, k * P:(k + 1) * P], m1[:, i, :],
                                      start=(i == 0), stop=(i == M1 // P - 1))
                m.then_inc(s_m2, 1)

            def mlp3(t, b):
                pe.wait_ge(s_m2c, t + 1)
                for i in range(M2 // P):
                    m = pe.matmul(b_r[b][0:1, 0:P], wt3[:, i:i + 1], m2[:, i, :], start=(i == 0), stop=(i == M2 // P - 1))
                m.then_inc(s_m3, 1)

            def run(name, i, t, par, b):
                if name == "T":
                    transpose_emb(t, par, i, b)
                elif name == "XT":
                    transpose_x(t, par, i, b)
                elif name == "HT":
                    transpose_h1(t, i, b)
                elif name == "G":
                    if i % 2 == 1:
                        contract_d(t, par, i - 1, ((b - 1) % 4, b))
                elif name in ("L2", "L2+"):
                    layer2(t, i, b)
                elif name == "m1":
                    mlp1(t, b)
                elif name == "m2":
                    mlp2(t, b)
                else:
                    mlp3(t, b)

            def wait_free(n, t, has1, has2, more):
                for m in range(n - 4, -1, -4):
                    if present(jobs[m][0], has1, has2, more):
                        name, i = jobs[m]
                        pe.wait_ge(copied[name], PER[name] * (t + TILE_OF[name]) + i + 1)
                        return
                for m in range(len(jobs) - 4 + (n - len(jobs)) % 4, -1, -4):
                    if has1 and present(jobs[m][0], has2, False, True):
                        name, i = jobs[m]
                        pe.wait_ge(copied[name], PER[name] * (t - 1 + TILE_OF[name]) + i + 1)
                        return

            def tile(t, par, has1, has2, more):
                for name, i in steps:
                    if name == "L1":
                        layer1(t, i, has1)
                        continue
                    if not present(name, has1, has2, more):
                        continue
                    if name not in BANKLESS:
                        wait_free(jobs.index((name, i)), t, has1, has2, more)
                    b = own_bank(name, i, bank_of)
                    run(name, i, t + TILE_OF[name], par ^ (TILE_OF[name] & 1), b)

            def tail():
                last = {bank_of[job]: job for job in jobs if job[0] != "T"}
                users = {b: (copied[n], PER[n] * (TILES - 1 + TILE_OF[n]) + i + 1) for b, (n, i) in last.items()}
                for name, i in tail_steps:
                    t, b = TILES - 1 + (i if name[0] == "m" else 0), own_bank(name, i, tail_bank)
                    if name not in BANKLESS:
                        pe.wait_ge(*users[b])
                        users[b] = (copied[name], PER[name] * t + (0 if name[0] == "m" else i) + 1)
                    run(name, i, t, 1, b)

            for k in range(4):
                transpose_emb(0, 0, k, bank_of["T", k])
            over_tiles(pe, tile, tail)


TABLES = [f"tbl_{f}" for f in range(39)]
_INS = ["dense_ctx", "ids"] + TABLES + ["W_top1", "b_top1", "W_top2", "b_top2", "W_top3", "L0_rec_W0", "L0_rec_W1"]


def kernel(**inputs):
    import numpy as _np
    import concourse.bacc as _bacc
    from concourse import mybir as _mybir
    from concourse.bass_utils import run_bass_kernel_spmd as _run

    nc = _bacc.Bacc("TRN2", target_bir_lowering=False, num_devices=1)
    arrays, a = {}, {}
    for name in _INS:
        x = _np.ascontiguousarray(inputs[name])
        arrays[f"in_{name}"] = x
        a[name] = nc.dram_tensor(f"in_{name}", x.shape, _mybir.dt.from_np(x.dtype), kind="ExternalInput").ap()
    n = inputs["ids"].shape[0]
    out = nc.dram_tensor("out_y", (n, 1), _mybir.dt.float32, kind="ExternalOutput").ap()
    build(nc, a["dense_ctx"], a["ids"], [a[t] for t in TABLES], a["W_top1"], a["b_top1"], a["W_top2"], a["b_top2"],
          a["W_top3"], a["L0_rec_W0"], a["L0_rec_W1"], out)
    r = _run(nc, [arrays], core_ids=[0])
    return r.results[0]["out_y"]
```
